# Optimizing a Trainium2 kernel written in Bass

```python
import numpy as np
import jax
import jax.numpy as jnp

def _softmax(x, axis=-1):
    return jax.nn.softmax(x, axis=axis)
def _gelu(x):
    return jax.nn.gelu(x, approximate=True)
def _silu(x):
    return jax.nn.silu(x)
def _sigmoid(x):
    return jax.nn.sigmoid(x)
def _layernorm(x, axis=-1, eps=1e-5):
    m = jnp.mean(x, axis=axis, keepdims=True)
    v = jnp.var(x, axis=axis, keepdims=True)
    return (x - m) / jnp.sqrt(v + eps)
def _scatter_add(tgt, idx, src, axis=0):
    return tgt.at[idx].add(src)
def _segment_sum(src, seg, n):
    return jax.ops.segment_sum(src, seg, n)

kernel_name = 'mk_conv_preact_d1_conv_nchw256_294fd3'

def setup_inputs(seed: int = 0):
    np.random.seed(seed)
    _w = jnp.asarray
    def _rec_inputs():
        import jax
        import jax.numpy as jnp
        _gk = jax.random.key(seed)
        x = -0.000125 + 0.9999 * jax.random.normal(jax.random.fold_in(_gk, 1), (32, 256, 64, 64), jnp.float32)
        return x
    x = _rec_inputs()
    def _L0_conv_setup():
        import jax, jax.numpy as jnp
        import numpy as np
        K = 3
        key = jax.random.key(seed)
        k1, k2 = jax.random.split(key)
        B, CIN, COUT, L = (32, 256, 256, 64)
        x = jax.random.normal(k1, (B, CIN, L, L), dtype=jnp.float32)
        rng = jnp.sqrt(jnp.asarray(1.0 / (CIN * K * K), dtype=jnp.float32))
        weight = (jax.random.uniform(k2, (COUT, CIN, K, K), dtype=jnp.float32) - 0.5) * 2.0 * rng
        return {'x': x, 'weight': weight}
    _L0_conv_all = _L0_conv_setup()
    _L0_conv_in = {k: v for k, v in _L0_conv_all.items() if k in ('weight', )}
    del _L0_conv_all

    return {
        "x": x,
        "L0_conv_weight": _L0_conv_in["weight"],
    }

def reference(x, L0_conv_weight):
    import jax
    import jax.numpy as jnp
    def _L0_conv_ref(x, weight):
        import jax, jax.numpy as jnp
        import numpy as np
        K = 3
        pad = K // 2
        L = x.shape[-1]
        LL = L + pad
        x_hat = jnp.fft.rfftn(x, s=(LL, LL), axes=(-2, -1))
        w_hat = jnp.fft.rfftn(weight[:, :, ::-1, ::-1], s=(LL, LL), axes=(-2, -1))
        res = jnp.einsum('bihw,oihw->bohw', x_hat, w_hat)
        out = jnp.fft.irfftn(res, s=(LL, LL), axes=(-2, -1))[:, :, pad:, pad:]
        return out

    def _gn(v, G=32, eps=1e-5):
        B_, C_, H_, W_ = v.shape
        g = v.reshape(B_, G, C_ // G, H_, W_)
        m = jnp.mean(g, axis=(2, 3, 4), keepdims=True)
        s = jnp.var(g, axis=(2, 3, 4), keepdims=True)
        return ((g - m) / jnp.sqrt(s + eps)).reshape(v.shape)

    def _ln_c(v, eps=1e-6):
        m = jnp.mean(v, axis=1, keepdims=True)
        s = jnp.var(v, axis=1, keepdims=True)
        return (v - m) / jnp.sqrt(s + eps)

    def _ln_t(v, eps=1e-5):
        m = jnp.mean(v, axis=-1, keepdims=True)
        s = jnp.var(v, axis=-1, keepdims=True)
        return (v - m) / jnp.sqrt(s + eps)

    def _to_tokens(v):
        B_, C_, H_, W_ = v.shape
        return v.reshape(B_, C_, H_ * W_).transpose(0, 2, 1)
    def _from_tokens(t, like):
        B_, C_, H_, W_ = like.shape
        return t.transpose(0, 2, 1).reshape(B_, C_, H_, W_)

    x = x + _L0_conv_ref(_gn(x), L0_conv_weight)
    return x


_drawn_inputs = setup_inputs


def setup_inputs(seed=0):
    import zlib

    import numpy as np

    out = dict(_drawn_inputs(seed))
    spreads = {}
    factors = {}
    for name, (base, spread) in spreads.items():
        noise = np.random.default_rng([zlib.crc32(name.encode()), seed]).standard_normal(out[name].shape)
        drawn = base * np.exp(spread * noise) if base else spread * noise
        out[name] = jnp.asarray(drawn.astype(out[name].dtype))
    for name, factor in factors.items():
        out[name] = (out[name] * factor).astype(out[name].dtype)
    return out
```

```python
import concourse.bass as bass
from concourse import mybir
from contextlib import ExitStack


def groupnorm_conv3x3_residual(nc: bass.Bass, x: bass.AP, weight: bass.AP, out: bass.AP):
    f32, f16, i32 = mybir.dt.float32, mybir.dt.float16, mybir.dt.int32
    ALU = mybir.AluOpType
    ACT = mybir.ActivationFunctionType
    AX = mybir.AxisListType

    IMAGES, C, H, W = x.shape
    P = 128
    CH = C // P
    GROUP = C // 32
    HALF = H // 2
    TILES = HALF // 4
    NPIX = TILES * W
    PIECE = HALF * W
    WP = W + 2
    PAIRS = ((1, 2), (3, 4), (0, 5))
    KW = 3
    UCOL = KW * CH * C
    GN_EPS = 1e-5
    ROW_SCALE = 32.0
    TAP_SCALE = 2.0 ** 14
    SETS = 3
    LAST = IMAGES - 1

    x_v = x.rearrange("n (c p) (h r) w -> n h c p (r w)", p=P, h=2)
    out_v = out.rearrange("n (c p) (h r) w -> n h c p (r w)", p=P, h=2)
    w_v = weight.rearrange("(c p) i a b -> c p (i a b)", p=P)

    with ExitStack() as ctx:
        def sb(name, shape, dt):
            return ctx.enter_context(nc.sbuf_tensor(name, shape, dt))

        def sem(name):
            return ctx.enter_context(nc.semaphore(name))

        xbuf = sb("xbuf", [P, 2, 2, CH, PIECE], f32)
        xn = sb("xn", [P, HALF + 4, CH, W], f32)
        diff = sb("diff", [P, TILES, 4, CH, W], f32)
        vrow = sb("vrow", [P, TILES, 2, CH, W], f32)
        v_hi = sb("v_hi", [P, 3, TILES, 2, CH, WP], f16)
        v_lo = sb("v_lo", [P, 3, TILES, 2, CH, WP], f16)
        u_hi = sb("u_hi", [P, 6, UCOL], f16)
        u_lo = sb("u_lo", [P, 6, UCOL], f16)
        wT = sb("wT", [P, 3, UCOL], f32)
        first = sb("first", [P, CH, 2, NPIX], f32)
        sumdiff = sb("sumdiff", [P, CH, TILES, 2, W], f32)
        junk = sb("junk", [P, PIECE], f16)
        ident = sb("ident", [P, P], f32)
        group_avg = sb("group_avg", [P, P], f32)
        zrow = sb("zrow", [P, CH * W], f32)
        sums = sb("sums", [P, 2, 2 * CH], f32)
        negmean = sb("negmean", [P, CH], f32)
        gn = sb("gn", [P, 4, CH], f32)
        gain = sb("gain", [P, CH], f32)
        shift = sb("shift", [P, CH], f32)
        wmax = sb("wmax", [P, CH], f32)
        wpow = sb("wpow", [P, CH], f32)
        expmask = sb("expmask", [P, CH], i32)
        wrec = sb("wrec", [P, CH], f32)
        unsc = sb("unsc", [P, 4, CH], f32)

        wbuf = xbuf[:, 1].rearrange("p h c n -> p (h c n)")
        wraw = wbuf[:, 0:CH * C * 9].rearrange("p (c n) -> p c n", c=CH)
        spare = CH * C * 9
        dflat = diff[:, :, :, :, :].rearrange("p t r c w -> p (t r c w)")
        mix = [wbuf[:, spare:spare + UCOL], wbuf[:, spare + UCOL:spare + 2 * UCOL],
               dflat[:, 0:UCOL], dflat[:, UCOL:2 * UCOL]]

        prod = ctx.enter_context(nc.psum_tensor("prod", [P, SETS, 2, NPIX], f32))
        stat = ctx.enter_context(nc.psum_tensor("stat", [P, 512], f32))
        wt_banks = prod[:, :, :, :].rearrange("p s b n -> p (s b) n")

        w_loaded = [sem(f"w_loaded{c}") for c in range(CH)]
        x_loaded = [[sem(f"x_loaded{h}{c}") for c in range(CH)] for h in range(2)]
        stored = [[sem(f"stored{h}{c}") for c in range(CH)] for h in range(2)]
        const_step = sem("const_step")
        const_ready = sem("const_ready")
        wscale_step = sem("wscale_step")
        w_scaled = sem("w_scaled")
        w_turned = sem("w_turned")
        wt_ready = sem("wt_ready")
        mixed = sem("mixed")
        u_hi_ready = sem("u_hi_ready")
        u_ready = sem("u_ready")
        sums_ready = sem("sums_ready")
        mean_ready = sem("mean_ready")
        negmean_ready = sem("negmean_ready")
        squares_ready = sem("squares_ready")
        var_ready = sem("var_ready")
        variance_ready = sem("variance_ready")
        root_ready = sem("root_ready")
        gn_step = sem("gn_step")
        gain_ready = sem("gain_ready")
        norm_ready = sem("norm_ready")
        edge_copied = sem("edge_copied")
        pq_ready = sem("pq_ready")
        diff_ready = sem("diff_ready")
        vrow_ready = sem("vrow_ready")
        v_hi_ready = sem("v_hi_ready")
        v_ready = sem("v_ready")
        products_done = sem("products_done")
        first_ready = sem("first_ready")
        set_read = sem("set_read")
        norm_step = sem("norm_step")
        rows_added = sem("rows_added")
        fours_added = sem("fours_added")

        def wait_all(eng, *needs):
            needs = [(s, n) for s, n in needs if not isinstance(n, int) or n > 0]
            for s, n in needs:
                if not isinstance(n, int):
                    eng.lower_val(n)
            for s, n in needs:
                eng.wait_ge(s, n)

        block = ctx.enter_context(nc.Block())

        @block.sync
        def _(sp):
            def load(i, par, h, c):
                sp.dma_start(xbuf[:, par, h, c, :], x_v[i, h, c]).then_inc(x_loaded[h][c], 16)

            def image(i, par, more):
                for h in range(2):
                    for c in range(CH):
                        sp.wait_ge(set_read, 12 * i + 6 * h + 4 + c + 1)
                        sp.dma_start(out_v[i, h, c], xbuf[:, par, h, c, :]).then_inc(stored[h][c], 16)
                    for c in range(CH if more else 0):
                        wait_all(sp, (stored[h][c], 16 * i + 16), (x_loaded[h][c], 16 * i + 32))
                        load(i + 2, par, h, c)

            for c in range(CH):
                sp.dma_start(wraw[:, c, :], w_v[c]).then_inc(w_loaded[c], 16)
            for h in range(2):
                for c in range(CH):
                    load(0, 0, h, c)
            sp.wait_ge(u_ready, 6)
            for h in range(2):
                for c in range(CH):
                    sp.wait_ge(x_loaded[h][c], 16)
                    load(1, 1, h, c)
            with sp.Fori(0, IMAGES // 2 - 1) as two:
                image(2 * two, 0, True)
                image(2 * two + 1, 1, True)
            image(LAST - 1, 0, False)
            image(LAST, 1, False)
            for h in range(2):
                for c in range(CH):
                    sp.wait_ge(stored[h][c], 16 * IMAGES)

        @block.gpsimd
        def _(pool):
            pool.memset(ident[:, :], 0.0).then_inc(const_step, 1)
            pool.memset(group_avg[:, :], 1.0 / (GROUP * H * W)).then_inc(const_step, 1)
            pool.memset(zrow[:, :], 0.0)
            for v in (v_hi, v_lo):
                rows = v[:, :, :, :, :, :].rearrange("p s t j c w -> p (s t j c) w")
                pool.memset(rows[:, :, 0:WP:WP - 1], 0.0)
            pool.wait_ge(const_step, 2)
            pool.affine_select(out=ident[:, :], in_=ident[:, :], compare_op=ALU.not_equal, fill=1.0,
                               base=0, pattern=[[-1, P]], channel_multiplier=1).then_inc(const_step, 1)
            groups = group_avg[:, :].rearrange("p (g m) -> p g m", m=GROUP)
            pool.affine_select(out=groups, in_=groups, compare_op=ALU.is_ge, fill=0.0, base=0,
                               pattern=[[-GROUP, P // GROUP], [0, GROUP]],
                               channel_multiplier=1).then_inc(const_step, 1)
            pool.wait_ge(const_step, 4)
            pool.affine_select(out=groups, in_=groups, compare_op=ALU.is_ge, fill=0.0, base=GROUP - 1,
                               pattern=[[GROUP, P // GROUP], [0, GROUP]],
                               channel_multiplier=-1).then_inc(const_ready, 1)

        @block.scalar
        def _(act):
            def add_up(i, par, h, c):
                k = CH * h + c
                wait_all(act, (x_loaded[h][c], 16 * (i + 1)),
                         (sums_ready, 4 * i + k) if k else (squares_ready, 4 * i))
                nc.scalar.activation(junk[:, :], xbuf[:, par, h, c, :], ACT.Copy,
                                     accum_out=sums[:, 0, k:k + 1]).then_inc(sums_ready, 1)

            def square_up(i, par):
                for h in range(2):
                    for c in range(CH):
                        k = CH * h + c
                        wait_all(act, (squares_ready, 4 * i + k) if k else (negmean_ready, i + 1))
                        nc.scalar.activation(junk[:, :], xbuf[:, par, h, c, :], ACT.Square,
                                             bias=negmean[:, c:c + 1],
                                             accum_out=sums[:, 1, k:k + 1]).then_inc(squares_ready, 1)

            def normalise(i, par, h):
                if h == 1:
                    wait_all(act, (diff_ready, 2 * i + 1))
                if h == 0:
                    wait_all(act, (diff_ready, 2 * i), (variance_ready, i + 1))
                    nc.scalar.activation(gn[:, 1, :], gn[:, 0, :], ACT.Sqrt).then_inc(root_ready, 1)
                    act.wait_ge(gain_ready, i + 1)
                edge, other = (0, HALF + 1) if h == 0 else (HALF + 1, 0)
                flat = xn[:, :, :, :].rearrange("p r c w -> p r (c w)")
                if h == 1:
                    nc.scalar.activation(flat[:, other, :], flat[:, HALF, :],
                                         ACT.Copy).then_inc(edge_copied, 1)
                    act.wait_ge(edge_copied, i + 1)
                nc.scalar.activation(flat[:, edge, :], zrow[:, :], ACT.Copy)
                for c in range(CH):
                    rows = xbuf[:, par, h, c, :].rearrange("p (r w) -> p r w", w=W)
                    ins = nc.scalar.activation(xn[:, 1:HALF + 1, c, :], rows, ACT.Identity,
                                               bias=shift[:, c:c + 1], scale=gain[:, c:c + 1])
                    if h == 0:
                        ins = nc.scalar.activation(xn[:, other, c, :], xbuf[:, par, 1, c, 0:W],
                                                   ACT.Identity, bias=shift[:, c:c + 1],
                                                   scale=gain[:, c:c + 1])
                ins.then_inc(norm_ready, 1)

            def high_part(g, k):
                wait_all(act, (vrow_ready, g + 1), (products_done, 2 * g - 4))
                nc.scalar.activation(
                    v_hi[:, k, :, :, :, 1:W + 1].rearrange("p t j c w -> p (t j c) w"),
                    vrow[:, :, :, :, :].rearrange("p t j c w -> p (t j c) w"),
                    ACT.Copy).then_inc(v_hi_ready, 1)

            def copy_first(u, k, c):
                q = 6 * u + 2 * k + c
                if k == 2:
                    return
                bank = prod[:, q_set(k, c), 0, :]
                wait_all(act, (products_done, q + 1), (set_read, q - 3 if k == 0 else q - 1))
                ins = nc.scalar.activation(first[:, c, 0, :], bank, ACT.Copy, scale=unsc[:, 0, c:c + 1])
                if k == 1:
                    ins = nc.scalar.activation(first[:, c, 1, :], bank, ACT.Copy,
                                               scale=unsc[:, 1, c:c + 1])
                ins.then_inc(first_ready, 1)

            def high_weights(n, j, src, factor):
                if n < 4:
                    act.wait_ge(mixed, (3, 4, 5, 6)[n])
                nc.scalar.activation(u_hi[:, j, :], src, ACT.Copy, scale=factor).then_inc(u_hi_ready, 1)

            def image(i, par, last=False):
                for s in range(6):
                    u, k, g = 2 * i + s // 3, s % 3, 6 * i + s
                    copy_first(u, k, 0)
                    if s == 1:
                        normalise(i, par, 1)
                    if s == 4 and not last:
                        normalise(i + 1, 1 - par, 0)
                    copy_first(u, k, 1)
                    if not (last and s >= 4):
                        high_part(g + 2, (k + 2) % 3)
                    if not last:
                        if s == 1:
                            add_up(i + 1, 1 - par, 0, 0)
                            add_up(i + 1, 1 - par, 0, 1)
                        if s == 2:
                            add_up(i + 1, 1 - par, 1, 0)
                            add_up(i + 1, 1 - par, 1, 1)
                        if s == 3:
                            square_up(i + 1, 1 - par)

            act.wait_ge(const_ready, 1)
            wT_taps = wT[:, :, :].rearrange("p a (b n) -> p (a b) n", b=KW)
            for tap in range(9):
                act.wait_ge(w_turned, tap + 1)
                nc.scalar.activation(wT_taps[:, tap, :], wt_banks[:, tap % 6, :],
                                     ACT.Copy).then_inc(wt_ready, 1)
            for c in range(CH):
                add_up(0, 0, 0, c)
            high_weights(0, 1, mix[0], -1.0 / 6)
            high_weights(1, 2, mix[1], -1.0 / 6)
            for c in range(CH):
                add_up(0, 0, 1, c)
            high_weights(2, 3, mix[2], 1.0 / 24)
            high_weights(3, 4, mix[3], 1.0 / 24)
            square_up(0, 0)
            high_weights(4, 0, wT[:, 0, :], 0.25)
            high_weights(5, 5, wT[:, 2, :], 1.0)
            normalise(0, 0, 0)
            high_part(0, 0)
            high_part(1, 1)
            image(0, 0)
            with act.Fori(0, IMAGES // 2 - 1) as two:
                image(2 * two + 1, 1)
                image(2 * two + 2, 0)
            image(LAST, 1, last=True)

        @block.tensor
        def _(pe):
            def product_set(i, s, c, wait_weights=False):
                q = 12 * i + 2 * s + c
                k = s % 3
                if wait_weights:
                    pe.wait_ge(u_ready, 2 * (k + 1))
                wait_all(pe, (v_ready, 6 * i + s + 1 if c == 0 else 0), (set_read, q - SETS + 1))
                for b, j in enumerate(PAIRS[k]):
                    n = 0
                    for ci in range(CH):
                        for kw in range(KW):
                            col = (kw * CH + ci) * C + c * P
                            for u, v in ((u_hi, v_hi), (u_hi, v_lo), (u_lo, v_hi)):
                                ins = nc.tensor.matmul(prod[:, q_set(k, c), b, :], u[:, j, col:col + P],
                                                       v[:, k, :, b, ci, kw:kw + W],
                                                       start=(n == 0), stop=(n == 3 * KW * CH - 1))
                                n += 1
                ins.then_inc(products_done, 1)

            def group_mean(i):
                wait_all(pe, (sums_ready, 4 * i + 4), (gain_ready, i))
                for h in range(2):
                    ins = nc.tensor.matmul(stat[:, 0:CH], group_avg[:, :], sums[:, 0, CH * h:CH * h + CH],
                                           start=(h == 0), stop=(h == 1))
                ins.then_inc(mean_ready, 1)

            def group_var(i):
                pe.wait_ge(squares_ready, 4 * i + 4)
                for h in range(2):
                    ins = nc.tensor.matmul(stat[:, CH:2 * CH], group_avg[:, :],
                                           sums[:, 1, CH * h:CH * h + CH], start=(h == 0), stop=(h == 1))
                ins.then_inc(var_ready, 1)

            def image(i, last=False, first=False):
                for s in range(6):
                    for c in range(CH):
                        product_set(i, s, c, wait_weights=first and s < 3 and c == 0)
                        if s == 3 and c == 0 and not last:
                            group_mean(i + 1)
                        if s == 4 and c == 0 and not last:
                            group_var(i + 1)

            pe.wait_ge(const_ready, 1)
            for tap in range(9):
                if tap >= 6:
                    pe.wait_ge(wt_ready, tap - 5)
                for c in range(CH):
                    if tap == 0:
                        pe.wait_ge(w_scaled, c + 1)
                    for ci in range(CH):
                        src = wraw[:, c, :].rearrange("p (i t) -> p i t", t=9)[:, ci * P:ci * P + P, tap]
                        ins = nc.tensor.transpose(
                            wt_banks[:, tap % 6, ci * C + c * P:ci * C + c * P + P], src, ident[:, :])
                ins.then_inc(w_turned, 1)
            group_mean(0)
            group_var(0)
            pe.wait_ge(wt_ready, 9)
            image(0, first=True)
            with pe.Fori(1, LAST) as i:
                image(i)
            image(LAST, last=True)

        @block.vector
        def _(dve):
            def centre(i):
                dve.wait_ge(mean_ready, i + 1)
                nc.vector.tensor_scalar(negmean[:, :], stat[:, 0:CH], -1.0, None,
                                        ALU.mult).then_inc(negmean_ready, 1)

            GN_STEPS = 4

            def variance(i):
                wait_all(dve, (var_ready, i + 1), (norm_ready, 2 * i))
                nc.vector.tensor_scalar(gn[:, 0, :], stat[:, CH:2 * CH], GN_EPS, None,
                                        ALU.add).then_inc(variance_ready, 1)

            def make_gain(i):
                step = GN_STEPS * i
                var, root, y, t = (gn[:, n, :] for n in range(4))
                dve.wait_ge(root_ready, i + 1)
                nc.vector.reciprocal(y, root).then_inc(gn_step, 1)
                dve.wait_ge(gn_step, step + 1)
                nc.vector.tensor_tensor(t, var, y, ALU.mult).then_inc(gn_step, 1)
                dve.wait_ge(gn_step, step + 2)
                nc.vector.tensor_tensor(root, t, y, ALU.mult).then_inc(gn_step, 1)
                dve.wait_ge(gn_step, step + 3)
                nc.vector.tensor_scalar(t, root, -0.5 * ROW_SCALE, 1.5 * ROW_SCALE, ALU.mult,
                                        ALU.add).then_inc(gn_step, 1)
                dve.wait_ge(gn_step, step + 4)
                nc.vector.tensor_tensor(gain[:, :], t, y, ALU.mult).then_inc(norm_step, 1)
                dve.wait_ge(norm_step, i + 1)
                nc.vector.tensor_tensor(shift[:, :], negmean[:, :], gain[:, :],
                                        ALU.mult).then_inc(gain_ready, 1)

            def transform(u, k):
                flat = xn[:, :, :, :].rearrange("p r c w -> p (r c w)")
                R = CH * W

                def rows(a, n):
                    return flat[:, a * R:(a + 4 * TILES) * R].rearrange(
                        "p (t m) -> p t m", t=TILES)[:, :, 0:n * R]

                def dif(a, n):
                    return diff[:, :, a:a + n, :, :].rearrange("p t r c w -> p t (r c w)")

                def vset(a, n):
                    return vrow[:, :, a:a + n, :, :].rearrange("p t j c w -> p t (j c w)")

                g = 3 * u + k
                if k == 0:
                    wait_all(dve, (norm_ready, u + 1), (vrow_ready, g))
                    nc.vector.scalar_tensor_tensor(dif(0, 2), rows(1, 2), -4.0, rows(3, 2), ALU.mult,
                                                   ALU.add).then_inc(pq_ready, 1)
                    wait_all(dve, (pq_ready, u + 1), (v_ready, g))
                    nc.vector.tensor_tensor(vset(0, 1), dif(1, 1), dif(0, 1), ALU.add)
                    nc.vector.tensor_tensor(vset(1, 1), dif(1, 1), dif(0, 1),
                                            ALU.subtract).then_inc(vrow_ready, 1)
                if k == 1:
                    dve.wait_ge(vrow_ready, g)
                    nc.vector.tensor_tensor(
                        diff[:, :, :, :, :].rearrange("p t r c w -> p (t r c w)"),
                        flat[:, 2 * R:(HALF + 2) * R], flat[:, 0:HALF * R],
                        ALU.subtract).then_inc(diff_ready, 1)
                    wait_all(dve, (diff_ready, u + 1), (v_ready, g))
                    nc.vector.scalar_tensor_tensor(vset(0, 1), dif(1, 1), 2.0, dif(2, 1), ALU.mult,
                                                   ALU.add)
                    nc.vector.scalar_tensor_tensor(vset(1, 1), dif(1, 1), -2.0, dif(2, 1), ALU.mult,
                                                   ALU.add).then_inc(vrow_ready, 1)
                if k == 2:
                    dve.wait_ge(v_ready, g)
                    nc.vector.scalar_tensor_tensor(vset(0, 2), dif(0, 2), -4.0, dif(2, 2), ALU.mult,
                                                   ALU.add).then_inc(vrow_ready, 1)

            def low_part(g, k):
                dve.wait_ge(v_hi_ready, g + 1)
                hi, lo = (v[:, k, :, :, :, 1:W + 1].rearrange("p t j c w -> p (t j c) w")
                          for v in (v_hi, v_lo))
                nc.vector.tensor_tensor(lo, vrow[:, :, :, :, :].rearrange("p t j c w -> p (t j c) w"),
                                        hi, ALU.subtract).then_inc(v_ready, 1)

            def gather(u, par, h, k, c):
                q = 6 * u + 2 * k + c
                xr = xbuf[:, par, h, c, :].rearrange("p (t r w) -> p t r w", r=4, w=W)
                x2 = xbuf[:, par, h, c, :].rearrange("p (t s m) -> p t s m", s=2, m=2 * W)
                m = [prod[:, q_set(k, c), b, :].rearrange("p (t w) -> p t w", w=W) for b in range(2)]
                f = [first[:, c, b, :].rearrange("p (t w) -> p t w", w=W) for b in range(2)]
                sd = sumdiff[:, c, :, :, :].rearrange("p t b w -> p t (b w)")
                pos, neg, neg2 = (unsc[:, n, c:c + 1] for n in (0, 2, 3))
                if k < 2:
                    wait_all(dve, (first_ready, 4 * u + 2 * k + c + 1),
                             (fours_added, 2 * u + c - 1) if k == 0 else (rows_added, 2 * u + c + 1))
                    nc.vector.scalar_tensor_tensor(sumdiff[:, c, :, 0, :], m[1], pos, f[0], ALU.mult,
                                                   ALU.add)
                    nc.vector.scalar_tensor_tensor(sumdiff[:, c, :, 1, :], m[1], neg if k == 0 else neg2,
                                                   f[k], ALU.mult, ALU.add).then_inc(set_read, 1)
                if k == 0:
                    dve.wait_ge(set_read, q + 1)
                    both = sd.unsqueeze(2).broadcast_to([P, TILES, 2, 2 * W])
                    nc.vector.tensor_tensor(x2, x2, both, ALU.add).then_inc(rows_added, 1)
                if k == 1:
                    dve.wait_ge(set_read, q + 1)
                    nc.vector.tensor_tensor(x2[:, :, 0, :], x2[:, :, 0, :], sd, ALU.add)
                    nc.vector.scalar_tensor_tensor(x2[:, :, 1, :], sd, 4.0, x2[:, :, 1, :], ALU.mult,
                                                   ALU.add).then_inc(fours_added, 1)
                if k == 2:
                    wait_all(dve, (products_done, q + 1), (fours_added, 2 * u + c + 1))
                    nc.vector.scalar_tensor_tensor(xr[:, :, 0, :], m[0], pos, xr[:, :, 0, :], ALU.mult,
                                                   ALU.add)
                    nc.vector.scalar_tensor_tensor(xr[:, :, 3, :], m[1], pos, xr[:, :, 3, :], ALU.mult,
                                                   ALU.add).then_inc(set_read, 1)

            def image(i, par, last=False):
                for s in range(6):
                    u, h, k, g = 2 * i + s // 3, s // 3, s % 3, 6 * i + s
                    if s == 4 and not last:
                        variance(i + 1)
                    gather(u, par, h, k, 0)
                    if s == 4 and not last:
                        make_gain(i + 1)
                    if s == 3 and not last:
                        centre(i + 1)
                    ahead = not (last and s >= 4)
                    if ahead:
                        transform(2 * i + (s + 2) // 3, (k + 2) % 3)
                    gather(u, par, h, k, 1)
                    if ahead:
                        low_part(g + 2, (k + 2) % 3)

            nc.vector.memset(expmask[:, :], 0x7F800000).then_inc(wscale_step, 1)
            for c in range(CH):
                dve.wait_ge(w_loaded[c], 16)
                nc.vector.tensor_reduce(wmax[:, c:c + 1], wraw[:, c, :], AX.X, ALU.max,
                                        apply_absolute_value=True).then_inc(wscale_step, 1)
            dve.wait_ge(wscale_step, 3)
            nc.vector.tensor_tensor(wpow[:, :].bitcast(i32), wmax[:, :].bitcast(i32), expmask[:, :],
                                    ALU.bitwise_and).then_inc(wscale_step, 1)
            dve.wait_ge(wscale_step, 4)
            nc.vector.tensor_scalar(wmax[:, :], wpow[:, :], 2.0 ** -100, None,
                                    ALU.max).then_inc(wscale_step, 1)
            dve.wait_ge(wscale_step, 5)
            nc.vector.reciprocal(wrec[:, :], wmax[:, :]).then_inc(wscale_step, 1)
            for n, sign in enumerate((1.0, 2.0, -1.0, -2.0)):
                nc.vector.tensor_scalar(unsc[:, n, :], wmax[:, :], sign / (TAP_SCALE * ROW_SCALE), None,
                                        ALU.mult).then_inc(wscale_step, 1)
            dve.wait_ge(wscale_step, 10)
            for c in range(CH):
                nc.vector.tensor_scalar(wraw[:, c, :], wraw[:, c, :], wrec[:, c:c + 1], TAP_SCALE,
                                        ALU.mult, ALU.mult).then_inc(w_scaled, 1)

            def low_weights(n, j, src, factor):
                dve.wait_ge(u_hi_ready, n + 1)
                nc.vector.scalar_tensor_tensor(u_lo[:, j, :], src, factor, u_hi[:, j, :], ALU.mult,
                                               ALU.subtract).then_inc(u_ready, 1)

            dve.wait_ge(wt_ready, 9)
            w0, w1, w2 = (wT[:, a, :] for a in range(3))
            nc.vector.tensor_tensor(mix[2], w0, w2, ALU.add).then_inc(mixed, 1)
            nc.vector.scalar_tensor_tensor(mix[3], w2, 4.0, w0, ALU.mult, ALU.add).then_inc(mixed, 1)
            dve.wait_ge(mixed, 2)
            nc.vector.tensor_tensor(mix[0], mix[2], w1, ALU.add).then_inc(mixed, 1)
            nc.vector.tensor_tensor(mix[1], mix[2], w1, ALU.subtract).then_inc(mixed, 1)
            dve.wait_ge(mixed, 4)
            nc.vector.scalar_tensor_tensor(mix[2], w1, 2.0, mix[3], ALU.mult, ALU.add).then_inc(mixed, 1)
            dve.wait_ge(mixed, 5)
            nc.vector.scalar_tensor_tensor(mix[3], w1, -2.0, mix[3], ALU.mult, ALU.add).then_inc(mixed, 1)
            low_weights(0, 1, mix[0], -1.0 / 6)
            low_weights(1, 2, mix[1], -1.0 / 6)
            dve.wait_ge(mixed, 6)
            low_weights(2, 3, mix[2], 1.0 / 24)
            low_weights(3, 4, mix[3], 1.0 / 24)
            centre(0)
            low_weights(4, 0, w0, 0.25)
            low_weights(5, 5, w2, 1.0)
            dve.wait_ge(u_ready, 6)
            variance(0)
            make_gain(0)
            transform(0, 0)
            low_part(0, 0)
            transform(0, 1)
            low_part(1, 1)
            image(0, 0)
            with dve.Fori(0, IMAGES // 2 - 1) as two:
                image(2 * two + 1, 1)
                image(2 * two + 2, 0)
            image(LAST, 1, last=True)


def q_set(k, c):
    return (2 * k + c) % 3


_INS = ['x', 'L0_conv_weight']
_OUTS = [((32, 256, 64, 64), 'float32')]


def kernel(**inputs):
    import numpy as _np
    import concourse.bacc as _bacc
    from concourse import mybir as _mybir
    from concourse.bass_utils import run_bass_kernel_spmd as _run

    nc = _bacc.Bacc("TRN2", target_bir_lowering=False, num_devices=1)
    arrays, args = {}, []
    for name in _INS:
        a = _np.ascontiguousarray(inputs[name])
        arrays[f"in_{name}_dram"] = a
        args.append(nc.dram_tensor(f"in_{name}_dram", a.shape, _mybir.dt.from_np(a.dtype), kind="ExternalInput").ap())
    for i, (shape, dtype) in enumerate(_OUTS):
        dt = _mybir.dt.from_np(_np.dtype(dtype))
        args.append(nc.dram_tensor(f"out_{i}_dram", shape, dt, kind="ExternalOutput").ap())
    groupnorm_conv3x3_residual(nc, *args)
    r = _run(nc, [arrays], core_ids=[0])
    got = tuple(r.results[0][f"out_{i}_dram"] for i in range(len(_OUTS)))
    return got[0]
```

```python
import concourse.bass as bass
from concourse import mybir
from contextlib import ExitStack


def groupnorm_conv3x3_residual(nc: bass.Bass, x: bass.AP, weight: bass.AP, out: bass.AP):
    f32, f16, i32 = mybir.dt.float32, mybir.dt.float16, mybir.dt.int32
    ALU = mybir.AluOpType
    ACT = mybir.ActivationFunctionType
    AX = mybir.AxisListType

    IMAGES, C, H, W = x.shape
    P = 128
    CH = C // P
    GROUP = C // 32
    HALF = H // 2
    TILES = HALF // 4
    NPIX = TILES * W
    PIECE = HALF * W
    PAIRS = ((1, 2), (3, 4), (0, 5))
    KW = 3
    UCOL = KW * CH * C
    GN_EPS = 1e-5
    ROW_SCALE = 32.0
    TAP_SCALE = 2.0 ** 14
    SETS = 3
    LAST = IMAGES - 1

    x_v = x.rearrange("n (c p) (h r) w -> n h c p (r w)", p=P, h=2)
    out_v = out.rearrange("n (c p) (h r) w -> n h c p (r w)", p=P, h=2)
    w_v = weight.rearrange("(c p) i a b -> c p (i a b)", p=P)

    with ExitStack() as ctx:
        def sb(name, shape, dt):
            return ctx.enter_context(nc.sbuf_tensor(name, shape, dt))

        def sem(name):
            return ctx.enter_context(nc.semaphore(name))

        xbuf = sb("xbuf", [P, 2, 2, CH, PIECE], f32)
        xn = sb("xn", [P, HALF + 4, CH, W], f32)
        diff = sb("diff", [P, TILES, 4, CH, W], f32)
        vrow = sb("vrow", [P, TILES, 2, CH, W], f32)
        v_hi = sb("v_hi", [P, 3, TILES, 2, CH, W], f16)
        v_lo = sb("v_lo", [P, 3, TILES, 2, CH, W], f16)
        u_hi = sb("u_hi", [P, 6, UCOL], f16)
        u_lo = sb("u_lo", [P, 6, UCOL], f16)
        w_row0 = sb("w_row0", [P, UCOL], f32)
        w_row2 = sb("w_row2", [P, UCOL], f32)
        first = sb("first", [P, CH, 2, NPIX], f32)
        sumdiff = sb("sumdiff", [P, CH, TILES, 2, W], f32)
        junk = sb("junk", [P, 2, PIECE], f16)
        ident = sb("ident", [P, P], f32)
        group_avg = sb("group_avg", [P, P], f32)
        zrow = sb("zrow", [P, CH * W], f32)
        sums = sb("sums", [P, 2, CH], f32)
        negmean = sb("negmean", [P, CH], f32)
        gn = sb("gn", [P, 4, CH], f32)
        gain = sb("gain", [P, CH], f32)
        shift = sb("shift", [P, CH], f32)
        wmax = sb("wmax", [P, CH], f32)
        wpow = sb("wpow", [P, CH], f32)
        expmask = sb("expmask", [P, CH], i32)
        wrec = sb("wrec", [P, CH], f32)
        unsc = sb("unsc", [P, 4, CH], f32)

        wT = [w_row0[:, :], sumdiff[:, :, :, :, :].rearrange("p c t b w -> p (c t b w)")[:, 0:UCOL],
              w_row2[:, :]]
        wbuf = xbuf[:, 1].rearrange("p h c n -> p (h c n)")
        wraw = wbuf[:, 0:CH * C * 9].rearrange("p (c n) -> p c n", c=CH)
        mix = [wbuf[:, n * UCOL:(n + 1) * UCOL] for n in range(4)]

        prod = ctx.enter_context(nc.psum_tensor("prod", [P, SETS, 2, NPIX], f32))
        stat = ctx.enter_context(nc.psum_tensor("stat", [P, 512], f32))
        wt_banks = prod[:, :, :, :].rearrange("p s b n -> p (s b) n")

        w_loaded = [sem(f"w_loaded{c}") for c in range(CH)]
        x_loaded = [[sem(f"x_loaded{h}{c}") for c in range(CH)] for h in range(2)]
        stored = [[sem(f"stored{h}{c}") for c in range(CH)] for h in range(2)]
        const_step = sem("const_step")
        const_ready = sem("const_ready")
        wscale_step = sem("wscale_step")
        w_scaled = sem("w_scaled")
        w_turned = sem("w_turned")
        wt_ready = sem("wt_ready")
        mixed = sem("mixed")
        u_hi_ready = sem("u_hi_ready")
        u_ready = sem("u_ready")
        table_ready = sem("table_ready")
        sums_ready = sem("sums_ready")
        mean_ready = sem("mean_ready")
        negmean_ready = sem("negmean_ready")
        squares_ready = sem("squares_ready")
        var_ready = sem("var_ready")
        variance_ready = sem("variance_ready")
        root_ready = sem("root_ready")
        gn_step = sem("gn_step")
        gain_made = sem("gain_made")
        gain_ready = sem("gain_ready")
        norm_ready = sem("norm_ready")
        edge_copied = sem("edge_copied")
        pq_ready = sem("pq_ready")
        diff_ready = sem("diff_ready")
        vrow_ready = sem("vrow_ready")
        v_hi_ready = sem("v_hi_ready")
        v_ready = sem("v_ready")
        products_done = sem("products_done")
        first_ready = sem("first_ready")
        set_read = sem("set_read")
        rows_added = sem("rows_added")
        fours_added = sem("fours_added")

        def wait_all(eng, *needs):
            needs = [(s, n) for s, n in needs if not isinstance(n, int) or n > 0]
            for s, n in needs:
                if not isinstance(n, int):
                    eng.lower_val(n)
            for s, n in needs:
                eng.wait_ge(s, n)

        block = ctx.enter_context(nc.Block())

        @block.sync
        def _(sp):
            def load(i, par, h, c):
                sp.dma_start(xbuf[:, par, h, c, :], x_v[i, h, c]).then_inc(x_loaded[h][c], 16)

            def image(i, par, more):
                for h in range(2):
                    for c in range(CH):
                        sp.wait_ge(set_read, 12 * i + 6 * h + 4 + c + 1)
                        sp.dma_start(out_v[i, h, c], xbuf[:, par, h, c, :]).then_inc(stored[h][c], 16)
                    for c in range(CH if more else 0):
                        wait_all(sp, (stored[h][c], 16 * i + 16), (x_loaded[h][c], 16 * i + 32))
                        load(i + 2, par, h, c)

            for c in range(CH):
                sp.dma_start(wraw[:, c, :], w_v[c]).then_inc(w_loaded[c], 16)
            for c in range(CH):
                for h in range(2):
                    load(0, 0, h, c)
            sp.wait_ge(u_ready, 6)
            for h in range(2):
                for c in range(CH):
                    sp.wait_ge(x_loaded[h][c], 16)
                    load(1, 1, h, c)
            with sp.Fori(0, IMAGES // 2 - 1) as two:
                image(2 * two, 0, True)
                image(2 * two + 1, 1, True)
            image(LAST - 1, 0, False)
            image(LAST, 1, False)
            for h in range(2):
                for c in range(CH):
                    sp.wait_ge(stored[h][c], 16 * IMAGES)

        @block.gpsimd
        def _(pool):
            pool.memset(ident[:, :], 0.0).then_inc(const_step, 1)
            pool.memset(group_avg[:, :], 1.0 / (GROUP * H * W)).then_inc(const_step, 1)
            pool.memset(zrow[:, :], 0.0)
            pool.wait_ge(const_step, 2)
            pool.affine_select(out=ident[:, :], in_=ident[:, :], compare_op=ALU.not_equal, fill=1.0,
                               base=0, pattern=[[-1, P]], channel_multiplier=1).then_inc(const_step, 1)
            groups = group_avg[:, :].rearrange("p (g m) -> p g m", m=GROUP)
            pool.affine_select(out=groups, in_=groups, compare_op=ALU.is_ge, fill=0.0, base=0,
                               pattern=[[-GROUP, P // GROUP], [0, GROUP]],
                               channel_multiplier=1).then_inc(const_step, 1)
            pool.wait_ge(const_step, 4)
            pool.affine_select(out=groups, in_=groups, compare_op=ALU.is_ge, fill=0.0, base=GROUP - 1,
                               pattern=[[GROUP, P // GROUP], [0, GROUP]],
                               channel_multiplier=-1).then_inc(const_ready, 1)

        @block.scalar
        def _(act):
            def add_up(i, par):
                for c in range(CH):
                    wait_all(act, (x_loaded[0][c], 16 * (i + 1)), (x_loaded[1][c], 16 * (i + 1)),
                             (sums_ready, CH * i + c) if c else (squares_ready, CH * i))
                    nc.scalar.activation(junk[:, :, :], xbuf[:, par, :, c, :], ACT.Copy,
                                         accum_out=sums[:, 0, c:c + 1]).then_inc(sums_ready, 1)

            def square_up(i, par, c):
                wait_all(act, (squares_ready, CH * i + c) if c else (negmean_ready, i + 1))
                nc.scalar.activation(junk[:, :, :], xbuf[:, par, :, c, :], ACT.Square,
                                     bias=negmean[:, c:c + 1],
                                     accum_out=sums[:, 1, c:c + 1]).then_inc(squares_ready, 1)

            def root_up(i):
                act.wait_ge(variance_ready, i + 1)
                nc.scalar.activation(gn[:, 1, :], gn[:, 0, :], ACT.Sqrt).then_inc(root_ready, 1)

            def normalise(i, par, h):
                wait_all(act, (diff_ready, 2 * i + h), (gain_ready, i + 1 if h == 0 else 0))
                edge, other = (0, HALF + 1) if h == 0 else (HALF + 1, 0)
                flat = xn[:, :, :, :].rearrange("p r c w -> p r (c w)")
                if h == 1:
                    nc.scalar.activation(flat[:, other, :], flat[:, HALF, :],
                                         ACT.Copy).then_inc(edge_copied, 1)
                    act.wait_ge(edge_copied, i + 1)
                nc.scalar.activation(flat[:, edge, :], zrow[:, :], ACT.Copy)
                for c in range(CH):
                    rows = xbuf[:, par, h, c, :].rearrange("p (r w) -> p r w", w=W)
                    ins = nc.scalar.activation(xn[:, 1:HALF + 1, c, :], rows, ACT.Identity,
                                               bias=shift[:, c:c + 1], scale=gain[:, c:c + 1])
                    if h == 0:
                        ins = nc.scalar.activation(xn[:, other, c, :], xbuf[:, par, 1, c, 0:W],
                                                   ACT.Identity, bias=shift[:, c:c + 1],
                                                   scale=gain[:, c:c + 1])
                ins.then_inc(norm_ready, 1)

            def high_part(g, k):
                wait_all(act, (vrow_ready, g + 1), (products_done, 2 * g - 4))
                nc.scalar.activation(v_hi[:, k].rearrange("p t j c w -> p (t j c w)"),
                                     vrow[:, :, :, :, :].rearrange("p t j c w -> p (t j c w)"),
                                     ACT.Copy).then_inc(v_hi_ready, 1)

            def copy_first(u, k, c):
                q = 6 * u + 2 * k + c
                if k == 2:
                    return
                bank = prod[:, q_set(k, c), 0, :]
                wait_all(act, (products_done, q + 1), (set_read, q - 3 if k == 0 else q - 1))
                ins = nc.scalar.activation(first[:, c, 0, :], bank, ACT.Copy, scale=unsc[:, 0, c:c + 1])
                if k == 1:
                    ins = nc.scalar.activation(first[:, c, 1, :], bank, ACT.Copy,
                                               scale=unsc[:, 1, c:c + 1])
                ins.then_inc(first_ready, 1)

            def high_weights(n, j, src, factor):
                if n < 4:
                    act.wait_ge(mixed, (2, 3, 5, 6)[n])
                nc.scalar.activation(u_hi[:, j, :], src, ACT.Copy, scale=factor).then_inc(u_hi_ready, 1)

            def image(i, par, last=False):
                for s in range(6):
                    u, k, g = 2 * i + s // 3, s % 3, 6 * i + s
                    copy_first(u, k, 0)
                    if s == 3 and not last:
                        square_up(i + 1, 1 - par, 1)
                    copy_first(u, k, 1)
                    if not (last and s >= 4):
                        high_part(g + 2, (k + 2) % 3)
                    if s == 0:
                        normalise(i, par, 1)
                    if not last:
                        if s == 1:
                            add_up(i + 1, 1 - par)
                        if s == 2:
                            square_up(i + 1, 1 - par, 0)
                        if s == 3:
                            root_up(i + 1)
                            normalise(i + 1, 1 - par, 0)

            act.wait_ge(const_ready, 1)
            nc.scalar.activation(junk[:, 0, 0:1], zrow[:, 0:1], ACT.Sqrt).then_inc(table_ready, 1)
            act.wait_ge(table_ready, 1)
            add_up(0, 0)
            square_up(0, 0, 0)
            square_up(0, 0, 1)
            high_weights(0, 1, mix[1], -1.0 / 6)
            root_up(0)
            normalise(0, 0, 0)
            high_weights(1, 2, mix[2], -1.0 / 6)
            high_part(0, 0)
            high_weights(2, 3, mix[0], 1.0 / 24)
            high_weights(3, 4, mix[3], 1.0 / 24)
            high_part(1, 1)
            high_weights(4, 0, wT[0], 0.25)
            high_weights(5, 5, wT[2], 1.0)
            image(0, 0)
            with act.Fori(0, IMAGES // 2 - 1) as two:
                image(2 * two + 1, 1)
                image(2 * two + 2, 0)
            image(LAST, 1, last=True)

        @block.tensor
        def _(pe):
            def product_set(i, s, c, wait_weights=False):
                q = 12 * i + 2 * s + c
                k = s % 3
                if wait_weights:
                    pe.wait_ge(u_ready, 2 * (k + 1))
                wait_all(pe, (v_ready, 6 * i + s + 1 if c == 0 else 0), (set_read, q - SETS + 1))
                for b, j in enumerate(PAIRS[k]):
                    bank = prod[:, q_set(k, c), b, :].rearrange("p (t w) -> p t w", w=W)
                    n = 0
                    for kw in (1, 0, 2):
                        o0, o1 = max(0, 1 - kw), W - max(0, kw - 1)
                        for ci in range(CH):
                            col = (kw * CH + ci) * C + c * P
                            for u, v in ((u_hi, v_hi), (u_hi, v_lo), (u_lo, v_hi)):
                                ins = nc.tensor.matmul(bank[:, :, o0:o1], u[:, j, col:col + P],
                                                       v[:, k, :, b, ci, o0 + kw - 1:o1 + kw - 1],
                                                       start=(n == 0), stop=(n == 3 * KW * CH - 1))
                                n += 1
                ins.then_inc(products_done, 1)

            def group_mean(i):
                wait_all(pe, (sums_ready, CH * (i + 1)), (gain_ready, i))
                nc.tensor.matmul(stat[:, 0:CH], group_avg[:, :], sums[:, 0, :], start=True,
                                 stop=True).then_inc(mean_ready, 1)

            def group_var(i):
                pe.wait_ge(squares_ready, CH * (i + 1))
                nc.tensor.matmul(stat[:, CH:2 * CH], group_avg[:, :], sums[:, 1, :], start=True,
                                 stop=True).then_inc(var_ready, 1)

            def image(i, last=False, first=False):
                for s in range(6):
                    for c in range(CH):
                        product_set(i, s, c, wait_weights=first and s < 3 and c == 0)
                    if s == 2 and not last:
                        group_mean(i + 1)
                    if s == 3 and not last:
                        group_var(i + 1)

            pe.wait_ge(const_ready, 1)
            for tap in range(9):
                if tap >= 6:
                    pe.wait_ge(wt_ready, tap - 5)
                for c in range(CH):
                    if tap == 0:
                        pe.wait_ge(w_scaled, c + 1)
                    for ci in range(CH):
                        src = wraw[:, c, :].rearrange("p (i t) -> p i t", t=9)[:, ci * P:ci * P + P, tap]
                        ins = nc.tensor.transpose(
                            wt_banks[:, tap % 6, ci * C + c * P:ci * C + c * P + P], src, ident[:, :])
                ins.then_inc(w_turned, 1)
            group_mean(0)
            group_var(0)
            pe.wait_ge(wt_ready, 9)
            image(0, first=True)
            with pe.Fori(1, LAST) as i:
                image(i)
            image(LAST, last=True)

        @block.vector
        def _(dve):
            def centre(i):
                dve.wait_ge(mean_ready, i + 1)
                nc.vector.tensor_scalar(negmean[:, :], stat[:, 0:CH], -1.0, None,
                                        ALU.mult).then_inc(negmean_ready, 1)

            GN_STEPS = 4

            def variance(i):
                wait_all(dve, (var_ready, i + 1), (norm_ready, 2 * i))
                nc.vector.tensor_scalar(gn[:, 0, :], stat[:, CH:2 * CH], GN_EPS, None,
                                        ALU.add).then_inc(variance_ready, 1)

            def make_gain(i):
                step = GN_STEPS * i
                var, root, y, t = (gn[:, n, :] for n in range(4))
                dve.wait_ge(root_ready, i + 1)
                nc.vector.reciprocal(y, root).then_inc(gn_step, 1)
                dve.wait_ge(gn_step, step + 1)
                nc.vector.tensor_tensor(t, var, y, ALU.mult).then_inc(gn_step, 1)
                dve.wait_ge(gn_step, step + 2)
                nc.vector.tensor_tensor(root, t, y, ALU.mult).then_inc(gn_step, 1)
                dve.wait_ge(gn_step, step + 3)
                nc.vector.tensor_scalar(t, root, -0.5 * ROW_SCALE, 1.5 * ROW_SCALE, ALU.mult,
                                        ALU.add).then_inc(gn_step, 1)
                dve.wait_ge(gn_step, step + 4)
                nc.vector.tensor_tensor(gain[:, :], t, y, ALU.mult).then_inc(gain_made, 1)
                dve.wait_ge(gain_made, i + 1)
                nc.vector.tensor_tensor(shift[:, :], negmean[:, :], gain[:, :],
                                        ALU.mult).then_inc(gain_ready, 1)

            def transform(u, k):
                flat = xn[:, :, :, :].rearrange("p r c w -> p (r c w)")
                R = CH * W

                def rows(a, n):
                    return flat[:, a * R:(a + 4 * TILES) * R].rearrange(
                        "p (t m) -> p t m", t=TILES)[:, :, 0:n * R]

                def dif(a, n):
                    return diff[:, :, a:a + n, :, :].rearrange("p t r c w -> p t (r c w)")

                def vset(a, n):
                    return vrow[:, :, a:a + n, :, :].rearrange("p t j c w -> p t (j c w)")

                g = 3 * u + k
                if k == 0:
                    wait_all(dve, (norm_ready, u + 1), (vrow_ready, g))
                    nc.vector.scalar_tensor_tensor(dif(0, 2), rows(1, 2), -4.0, rows(3, 2), ALU.mult,
                                                   ALU.add).then_inc(pq_ready, 1)
                    wait_all(dve, (pq_ready, u + 1), (v_ready, g))
                    nc.vector.tensor_tensor(vset(0, 1), dif(1, 1), dif(0, 1), ALU.add)
                    nc.vector.tensor_tensor(vset(1, 1), dif(1, 1), dif(0, 1),
                                            ALU.subtract).then_inc(vrow_ready, 1)
                if k == 1:
                    dve.wait_ge(vrow_ready, g)
                    nc.vector.tensor_tensor(
                        diff[:, :, :, :, :].rearrange("p t r c w -> p (t r c w)"),
                        flat[:, 2 * R:(HALF + 2) * R], flat[:, 0:HALF * R],
                        ALU.subtract).then_inc(diff_ready, 1)
                    wait_all(dve, (diff_ready, u + 1), (v_ready, g))
                    nc.vector.scalar_tensor_tensor(vset(0, 1), dif(1, 1), 2.0, dif(2, 1), ALU.mult,
                                                   ALU.add)
                    nc.vector.scalar_tensor_tensor(vset(1, 1), dif(1, 1), -2.0, dif(2, 1), ALU.mult,
                                                   ALU.add).then_inc(vrow_ready, 1)
                if k == 2:
                    dve.wait_ge(v_ready, g)
                    nc.vector.scalar_tensor_tensor(vset(0, 2), dif(0, 2), -4.0, dif(2, 2), ALU.mult,
                                                   ALU.add).then_inc(vrow_ready, 1)

            def low_part(g, k):
                dve.wait_ge(v_hi_ready, g + 1)
                hi, lo = (v[:, k].rearrange("p t j c w -> p (t j c w)") for v in (v_hi, v_lo))
                nc.vector.tensor_tensor(lo, vrow[:, :, :, :, :].rearrange("p t j c w -> p (t j c w)"),
                                        hi, ALU.subtract).then_inc(v_ready, 1)

            def gather(u, par, h, k, c):
                q = 6 * u + 2 * k + c
                xr = xbuf[:, par, h, c, :].rearrange("p (t r w) -> p t r w", r=4, w=W)
                x2 = xbuf[:, par, h, c, :].rearrange("p (t s m) -> p t s m", s=2, m=2 * W)
                m = [prod[:, q_set(k, c), b, :].rearrange("p (t w) -> p t w", w=W) for b in range(2)]
                f = [first[:, c, b, :].rearrange("p (t w) -> p t w", w=W) for b in range(2)]
                sd = sumdiff[:, c, :, :, :].rearrange("p t b w -> p t (b w)")
                pos, neg, neg2 = (unsc[:, n, c:c + 1] for n in (0, 2, 3))
                if k < 2:
                    wait_all(dve, (first_ready, 4 * u + 2 * k + c + 1),
                             (fours_added, 2 * u + c - 1) if k == 0 else (rows_added, 2 * u + c + 1))
                    nc.vector.scalar_tensor_tensor(sumdiff[:, c, :, 0, :], m[1], pos, f[0], ALU.mult,
                                                   ALU.add)
                    nc.vector.scalar_tensor_tensor(sumdiff[:, c, :, 1, :], m[1], neg if k == 0 else neg2,
                                                   f[k], ALU.mult, ALU.add).then_inc(set_read, 1)
                if k == 0:
                    dve.wait_ge(set_read, q + 1)
                    both = sd.unsqueeze(2).broadcast_to([P, TILES, 2, 2 * W])
                    nc.vector.tensor_tensor(x2, x2, both, ALU.add).then_inc(rows_added, 1)
                if k == 1:
                    dve.wait_ge(set_read, q + 1)
                    nc.vector.tensor_tensor(x2[:, :, 0, :], x2[:, :, 0, :], sd, ALU.add)
                    nc.vector.scalar_tensor_tensor(x2[:, :, 1, :], sd, 4.0, x2[:, :, 1, :], ALU.mult,
                                                   ALU.add).then_inc(fours_added, 1)
                if k == 2:
                    wait_all(dve, (products_done, q + 1), (fours_added, 2 * u + c + 1))
                    nc.vector.scalar_tensor_tensor(xr[:, :, 0, :], m[0], pos, xr[:, :, 0, :], ALU.mult,
                                                   ALU.add)
                    nc.vector.scalar_tensor_tensor(xr[:, :, 3, :], m[1], pos, xr[:, :, 3, :], ALU.mult,
                                                   ALU.add).then_inc(set_read, 1)

            def image(i, par, last=False):
                for s in range(6):
                    u, h, k, g = 2 * i + s // 3, s // 3, s % 3, 6 * i + s
                    if s == 3 and not last:
                        centre(i + 1)
                    gather(u, par, h, k, 0)
                    ahead = not (last and s >= 4)
                    if ahead:
                        transform(2 * i + (s + 2) // 3, (k + 2) % 3)
                    gather(u, par, h, k, 1)
                    if s == 3 and not last:
                        variance(i + 1)
                    if ahead:
                        low_part(g + 2, (k + 2) % 3)
                    if s == 3 and not last:
                        make_gain(i + 1)

            nc.vector.memset(expmask[:, :], 0x7F800000).then_inc(wscale_step, 1)
            for c in range(CH):
                dve.wait_ge(w_loaded[c], 16)
                nc.vector.tensor_reduce(wmax[:, c:c + 1], wraw[:, c, :], AX.X, ALU.max,
                                        apply_absolute_value=True).then_inc(wscale_step, 1)
            dve.wait_ge(wscale_step, 3)
            nc.vector.tensor_tensor(wpow[:, :].bitcast(i32), wmax[:, :].bitcast(i32), expmask[:, :],
                                    ALU.bitwise_and).then_inc(wscale_step, 1)
            dve.wait_ge(wscale_step, 4)
            nc.vector.tensor_scalar(wmax[:, :], wpow[:, :], 2.0 ** -100, None,
                                    ALU.max).then_inc(wscale_step, 1)
            dve.wait_ge(wscale_step, 5)
            nc.vector.reciprocal(wrec[:, :], wmax[:, :]).then_inc(wscale_step, 1)
            for n, sign in enumerate((1.0, 2.0, -1.0, -2.0)):
                nc.vector.tensor_scalar(unsc[:, n, :], wmax[:, :], sign / (TAP_SCALE * ROW_SCALE), None,
                                        ALU.mult).then_inc(wscale_step, 1)
            dve.wait_ge(wscale_step, 10)
            for c in range(CH):
                nc.vector.tensor_scalar(wraw[:, c, :], wraw[:, c, :], wrec[:, c:c + 1], TAP_SCALE,
                                        ALU.mult, ALU.mult).then_inc(w_scaled, 1)

            def low_weights(n, j, src, factor):
                dve.wait_ge(u_hi_ready, n + 1)
                nc.vector.scalar_tensor_tensor(u_lo[:, j, :], src, factor, u_hi[:, j, :], ALU.mult,
                                               ALU.subtract).then_inc(u_ready, 1)

            for tap in range(9):
                dve.wait_ge(w_turned, tap + 1)
                a, b = divmod(tap, KW)
                nc.vector.tensor_copy(wT[a][:, b * CH * C:(b + 1) * CH * C],
                                      wt_banks[:, tap % 6, :]).then_inc(wt_ready, 1)
            dve.wait_ge(wt_ready, 9)
            w0, w1, w2 = wT
            nc.vector.tensor_tensor(mix[0], w0, w2, ALU.add).then_inc(mixed, 1)
            centre(0)
            dve.wait_ge(mixed, 1)
            nc.vector.tensor_tensor(mix[1], mix[0], w1, ALU.add).then_inc(mixed, 1)
            nc.vector.tensor_tensor(mix[2], mix[0], w1, ALU.subtract).then_inc(mixed, 1)
            nc.vector.scalar_tensor_tensor(mix[3], w2, 4.0, w0, ALU.mult, ALU.add).then_inc(mixed, 1)
            dve.wait_ge(mixed, 4)
            nc.vector.scalar_tensor_tensor(mix[0], w1, 2.0, mix[3], ALU.mult, ALU.add).then_inc(mixed, 1)
            variance(0)
            low_weights(0, 1, mix[1], -1.0 / 6)
            make_gain(0)
            dve.wait_ge(mixed, 5)
            nc.vector.scalar_tensor_tensor(mix[3], w1, -2.0, mix[3], ALU.mult, ALU.add).then_inc(mixed, 1)
            transform(0, 0)
            low_weights(1, 2, mix[2], -1.0 / 6)
            low_part(0, 0)
            transform(0, 1)
            low_weights(2, 3, mix[0], 1.0 / 24)
            low_weights(3, 4, mix[3], 1.0 / 24)
            low_part(1, 1)
            low_weights(4, 0, w0, 0.25)
            low_weights(5, 5, w2, 1.0)
            image(0, 0)
            with dve.Fori(0, IMAGES // 2 - 1) as two:
                image(2 * two + 1, 1)
                image(2 * two + 2, 0)
            image(LAST, 1, last=True)


def q_set(k, c):
    return (2 * k + c) % 3


_INS = ['x', 'L0_conv_weight']
_OUTS = [((32, 256, 64, 64), 'float32')]


def kernel(**inputs):
    import numpy as _np
    import concourse.bacc as _bacc
    from concourse import mybir as _mybir
    from concourse.bass_utils import run_bass_kernel_spmd as _run

    nc = _bacc.Bacc("TRN2", target_bir_lowering=False, num_devices=1)
    arrays, args = {}, []
    for name in _INS:
        a = _np.ascontiguousarray(inputs[name])
        arrays[f"in_{name}_dram"] = a
        args.append(nc.dram_tensor(f"in_{name}_dram", a.shape, _mybir.dt.from_np(a.dtype), kind="ExternalInput").ap())
    for i, (shape, dtype) in enumerate(_OUTS):
        dt = _mybir.dt.from_np(_np.dtype(dtype))
        args.append(nc.dram_tensor(f"out_{i}_dram", shape, dt, kind="ExternalOutput").ap())
    groupnorm_conv3x3_residual(nc, *args)
    r = _run(nc, [arrays], core_ids=[0])
    got = tuple(r.results[0][f"out_{i}_dram"] for i in range(len(_OUTS)))
    return got[0]
```
